# Optimizing a Trainium2 kernel written in Bass

```python
import numpy as np
import jax
import jax.numpy as jnp

def _softmax(x, axis=-1):
    return jax.nn.softmax(x, axis=axis)
def _gelu(x):
    return jax.nn.gelu(x, approximate=True)
def _silu(x):
    return jax.nn.silu(x)
def _sigmoid(x):
    return jax.nn.sigmoid(x)
def _layernorm(x, axis=-1, eps=1e-5):
    m = jnp.mean(x, axis=axis, keepdims=True)
    v = jnp.var(x, axis=axis, keepdims=True)
    return (x - m) / jnp.sqrt(v + eps)
def _scatter_add(tgt, idx, src, axis=0):
    return tgt.at[idx].add(src)
def _segment_sum(src, seg, n):
    return jax.ops.segment_sum(src, seg, n)

kernel_name = 'mk_adj_resnorm_d2_adj_128_ea44a4'

def setup_inputs(seed: int = 0):
    np.random.seed(seed)
    _w = jnp.asarray
    def _rec_inputs():
        import jax
        import jax.numpy as jnp
        _gk = jax.random.key(seed)
        x = -0.000929 + 1 * jax.random.normal(jax.random.fold_in(_gk, 1), (8192, 128), jnp.float32)
        _w = (1.0 + jnp.arange(8192, dtype=jnp.float32)) ** -0.5
        _w = _w / _w.mean()
        _pij = jnp.clip(0.000976562 * _w[:, None] * _w[None, :], 0.0, 1.0)
        _a = jax.random.uniform(jax.random.fold_in(_gk, 2), (8192, 8192)) < _pij
        _a = jnp.logical_or(_a, jnp.swapaxes(_a, -1, -2))
        _a = jnp.logical_or(_a, jnp.eye(8192, dtype=bool))
        _af = _a.astype(jnp.float32)
        _af = _af * jax.random.uniform(jax.random.fold_in(_gk, 3), (8192, 8192), jnp.float32, 0.05, 5.41998)
        adj = _af
        return x, adj
    x, adj = _rec_inputs()
    def _L0_gnn_setup():
        import jax, jax.numpy as jnp
        import numpy as np
        IN_F, OUT_F = (128, 128)
        R, LEV, N = (2, 2, 8192)
        JD = (R - 1) * LEV + 1
        key = jax.random.key(seed)
        ks = jax.random.split(key, 7)
        x = jax.random.normal(ks[0], (N, IN_F), dtype=jnp.float32)
        d_list = jax.random.uniform(ks[1], (JD, N), dtype=jnp.float32)
        U = jax.random.normal(ks[2], (N, N), dtype=jnp.float32)
        Vt = jax.random.normal(ks[3], (N, N), dtype=jnp.float32)
        bound = float(np.sqrt(6.0 / (IN_F + OUT_F)))
        weight = jax.random.uniform(ks[4], (IN_F, OUT_F), dtype=jnp.float32, minval=-bound, maxval=bound)
        filt = jax.random.uniform(ks[5], (JD, N), dtype=jnp.float32, minval=0.9, maxval=1.1)
        bias = jnp.zeros((OUT_F,), dtype=jnp.float32)
        return {'x': x, 'd_list': d_list, 'U': U, 'Vt': Vt, 'weight': weight, 'filt': filt, 'bias': bias}
    _L0_gnn_all = _L0_gnn_setup()
    _L0_gnn_in = {k: v for k, v in _L0_gnn_all.items() if k in ('d_list', 'weight', 'filt', 'bias', )}
    del _L0_gnn_all

    def _L1_gnn_setup():
        import jax, jax.numpy as jnp
        import numpy as np
        N, E, D = (8192, 8192, 128)
        key = jax.random.key(seed)
        k1, k2 = jax.random.split(key)
        X = jax.random.normal(k1, (N, D), dtype=jnp.float32)
        H = jax.random.uniform(k2, (N, E), dtype=jnp.float32)
        return {'X': X, 'H': H}
    _L1_gnn_all = _L1_gnn_setup()
    _L1_gnn_in = {k: v for k, v in _L1_gnn_all.items() if k in ()}
    del _L1_gnn_all

    return {
        "x": x,
        "adj": adj,
        "L0_gnn_d_list": _L0_gnn_in["d_list"],
        "L0_gnn_weight": _L0_gnn_in["weight"],
        "L0_gnn_filt": _L0_gnn_in["filt"],
        "L0_gnn_bias": _L0_gnn_in["bias"],
    }

def reference(x, adj, L0_gnn_d_list, L0_gnn_weight, L0_gnn_filt, L0_gnn_bias):
    import jax
    import jax.numpy as jnp
    def _L0_gnn_ref(x, d_list, U, Vt, weight, filt, bias):
        import jax, jax.numpy as jnp
        import numpy as np
        IN_F, OUT_F = (128, 128)
        R, LEV, N = (2, 2, 8192)
        JD = (R - 1) * LEV + 1
        xw = x @ weight
        Vxw = Vt @ xw
        scale = jnp.sum(d_list * filt * d_list, axis=0)
        out = U @ (scale[:, None] * Vxw)
        return out + bias

    def _L1_gnn_ref(X, H):
        import jax, jax.numpy as jnp
        import numpy as np
        N, E, D = (8192, 8192, 128)
        msg = jnp.matmul(H.T, X)
        inv_deg = 1.0 / H.sum(axis=0)
        inv_deg = jnp.where(jnp.isinf(inv_deg), 0.0, inv_deg)
        return msg * inv_deg[:, None]

    x = _layernorm(x + _L0_gnn_ref(x, L0_gnn_d_list, adj, adj, L0_gnn_weight, L0_gnn_filt, L0_gnn_bias), axis=-1)
    x = _layernorm(x + _L1_gnn_ref(x, adj), axis=-1)
    return x


_drawn_inputs = setup_inputs


def setup_inputs(seed=0):
    import zlib

    import numpy as np

    out = dict(_drawn_inputs(seed))
    spreads = {'L0_gnn_bias': (0.0, 0.1)}
    factors = {}
    for name, (base, spread) in spreads.items():
        noise = np.random.default_rng([zlib.crc32(name.encode()), seed]).standard_normal(out[name].shape)
        drawn = base * np.exp(spread * noise) if base else spread * noise
        out[name] = jnp.asarray(drawn.astype(out[name].dtype))
    for name, factor in factors.items():
        out[name] = (out[name] * factor).astype(out[name].dtype)
    return out
```

```python
from contextlib import ExitStack

import concourse.bass as bass
from concourse import mybir

F32 = mybir.dt.float32
F32R = mybir.dt.float32r
BF16 = mybir.dt.bfloat16
U32 = mybir.dt.uint32
ALU = mybir.AluOpType
ACT = mybir.ActivationFunctionType
AX = mybir.AxisListType

P = 128
CHUNK = 1024
BANK = 512
HALVES = CHUNK // BANK
TILES = CHUNK // P
PAIR = 2
UNITS = TILES // PAIR
UNIT = PAIR * CHUNK
LO_RING = 2
EPS = 1e-5
LARGEST_WITHOUT_INVERSE = 2.0 ** -128


def build(nc, x, xT, A, AT, d, filt, weight, bias, out):
    N = x.shape[0]
    NC = N // CHUNK
    T = N // P
    NR = d.shape[1]
    assert NC % 2 == 0 and NC >= 4

    A_units = A.rearrange("(j u two p) i -> j u p two i", u=UNITS, two=PAIR, p=P)
    AT_units = AT.rearrange("(j u two p) i -> j u p two i", u=UNITS, two=PAIR, p=P)
    x_chunks = x.rearrange("(c t p) f -> c p t f", t=TILES, p=P)
    out_chunks = out.rearrange("(c t p) f -> c p t f", t=TILES, p=P)

    def first_block(phase, I):
        if phase == 1:
            return NC * I
        if phase == 2:
            return NC * NC + NC * I - I * (I - 1) // 2
        return NC * NC + NC * (NC + 1) // 2 + NC * I

    with ExitStack() as ctx:
        def sb(name, shape, dt=F32):
            return ctx.enter_context(nc.sbuf_tensor(name, shape, dt))

        def sem(name):
            return ctx.enter_context(nc.semaphore(name))

        features = sb("features", [P, 2, N])
        partial = sb("partial", [P, N])
        raw = sb("raw", [P, UNITS, UNIT])
        hi = sb("hi", [P, UNITS, UNIT], F32R)
        lo = sb("lo", [P, LO_RING, UNIT], F32R)
        HB = TILES // 2 * P
        w_hi = sb("w_hi", [P, 2, 2, HB], F32R)
        w_lo = sb("w_lo", [P, 2, 2, HB], F32R)
        turn = sb("turn", [P, CHUNK])
        rows = sb("rows", [P, TILES, P])
        deg_parts = sb("deg_parts", [P, NC, T])
        inv_deg = sb("inv_deg", [P, T])
        no_inv = sb("no_inv", [P, T], U32)
        zero_col = sb("zero_col", [P, T])
        ones = sb("ones", [P, T])
        abs_deg = sb("abs_deg", [P, T])
        d_sb = sb("d_sb", [P, NR, T])
        filt_sb = sb("filt_sb", [P, NR, T])
        scale = sb("scale", [P, T])
        w_sb = sb("w_sb", [P, P])
        bias_sb = sb("bias_sb", [P, 1])
        ident = sb("ident", [P, P])
        zeros = sb("zeros", [P, BANK], BF16)
        stats = sb("stats", [P, TILES, 6])
        mean = sb("mean", [P, TILES])
        spread = sb("spread", [P, TILES])
        var = sb("var", [P, TILES])
        eps_sb = sb("eps_sb", [P, 1])
        std = sb("std", [P, TILES])
        rstd = sb("rstd", [P, TILES])
        newton = sb("newton", [P, TILES])
        main = [ctx.enter_context(nc.psum_tensor(f"main{p}", [P, HALVES, BANK], F32)) for p in range(2)]
        side = [ctx.enter_context(nc.psum_tensor(f"side{p}", [P, HALVES, BANK], F32)) for p in range(2)]

        xt_loaded = [sem(f"xt_loaded{c}") for c in range(NC)]
        small_loaded = sem("small_loaded")
        w_loaded = sem("w_loaded")
        consts_ready = sem("consts_ready")
        xw_summed = sem("xw_summed")
        xw_ready = sem("xw_ready")
        side_zeroed = sem("side_zeroed")
        scale_step = sem("scale_step")
        raw_loaded = [sem(f"raw_loaded{u}") for u in range(UNITS)]
        hi_ready = sem("hi_ready")
        lo_ready = sem("lo_ready")
        unit_done = sem("unit_done")
        w_hi_ready = sem("w_hi_ready")
        w_lo_ready = sem("w_lo_ready")
        turn_ready = sem("turn_ready")
        turned = sem("turned")
        released = sem("released")
        rows_moved = sem("rows_moved")
        norm_step = sem("norm_step")
        var_ready = sem("var_ready")
        std_ready = sem("std_ready")
        normed = sem("normed")
        deg_step = sem("deg_step")

        block = ctx.enter_context(nc.Block())

        def walk(eng, work, epilogue):

            def chunk1(I, par):
                first, _ = epilogue(1, I - 1, I - 1, 1 - par)
                work(1, I, I, NC * I, par, False, first)
                if not (isinstance(I, int) and I == NC - 1):
                    with eng.Fori(I + 1, NC) as J:
                        work(1, I, J, (NC - 1) * I + J, par, False, {})
                with eng.Fori(0, I) as J:
                    work(1, I, J, (NC - 1) * I + NC + J, par, True, {})

            work(1, 0, 0, 0, 0, False, {})
            with eng.Fori(1, NC) as J:
                work(1, 0, J, J, 0, False, {})
            with eng.Fori(0, NC // 2 - 1) as q:
                chunk1(2 * q + 1, 1)
                chunk1(2 * q + 2, 0)
            chunk1(NC - 1, 1)

            for I in range(NC):
                B = first_block(2, I)
                kind, chunk = (2, I - 1) if I else (1, NC - 1)
                first, second = epilogue(kind, chunk, NC + I - 1, (I + 1) % 2)
                work(2, I, I, B, I % 2, False, first)
                if I + 1 < NC:
                    work(2, I, I + 1, B + 1, I % 2, False, second)
                else:
                    for hook in second.values():
                        hook()
                if I + 2 < NC:
                    with eng.Fori(I + 2, NC) as J:
                        work(2, I, J, B - I + J, I % 2, False, {})

            def chunk3(I, par, kind):
                B = first_block(3, I)
                first, second = epilogue(kind, I - 1 if kind == 3 else NC - 1, 2 * NC + I - 1, 1 - par)
                work(3, I, 0, B, par, False, first)
                work(3, I, 1, B + 1, par, False, second)
                with eng.Fori(2, NC) as J:
                    work(3, I, J, B + J, par, False, {})

            chunk3(0, 0, 2)
            with eng.Fori(0, NC // 2 - 1) as q:
                chunk3(2 * q + 1, 1, 3)
                chunk3(2 * q + 2, 0, 3)
            chunk3(NC - 1, 1, 3)
            first, second = epilogue(3, NC - 1, 3 * NC - 1, 1)
            for hook in (*first.values(), *second.values()):
                hook()

        def is_first(B):
            return isinstance(B, int) and B == 0

        def operands(phase, dual):
            return slice(0, 2) if dual else slice(1, 2) if phase == 2 else slice(0, 1)

        @block.sync
        def _(sp):
            sp.dma_start(w_sb[:, :], weight).then_inc(w_loaded, 16)
            for c in range(NC):
                sp.dma_start(partial[:, c * CHUNK:(c + 1) * CHUNK],
                             xT[:, c * CHUNK:(c + 1) * CHUNK]).then_inc(xt_loaded[c], 16)

            def load(phase, I, J, B, par, dual, hooks):
                units = A_units if phase == 3 else AT_units
                for u in range(UNITS):
                    if not is_first(B):
                        sp.wait_ge(lo_ready, UNITS * B - UNITS + u + 1)
                    sp.dma_start(raw[:, u, :].rearrange("p (two i) -> p two i", two=PAIR),
                                 units[J, u, :, :, bass.ds(I * CHUNK, CHUNK)]).then_inc(raw_loaded[u], 16)

            walk(sp, load, lambda kind, chunk, m, par: ({}, {}))

        @block.gpsimd
        def _(pool):
            pool.memset(ident[:, :], 0.0).then_inc(consts_ready, 1)
            pool.wait_ge(consts_ready, 1)
            pool.affine_select(out=ident[:, :], in_=ident[:, :], compare_op=ALU.not_equal, fill=1.0,
                               base=0, pattern=[[-1, P]], channel_multiplier=1).then_inc(consts_ready, 1)
            pool.memset(zeros[:, :], 0.0).then_inc(consts_ready, 1)
            pool.memset(eps_sb[:, :], EPS).then_inc(consts_ready, 1)
            pool.memset(zero_col[:, :], 0.0).then_inc(consts_ready, 1)
            pool.memset(ones[:, :], 1.0).then_inc(consts_ready, 1)
            pool.dma_start(d_sb[:, :, :], d).then_inc(small_loaded, 16)
            pool.dma_start(filt_sb[:, :, :], filt).then_inc(small_loaded, 16)
            pool.dma_start(bias_sb[:, :], bias).then_inc(small_loaded, 16)
            pool.dma_start(rows[:, :, :], x_chunks[0]).then_inc(rows_moved, 16)
            with pool.Fori(1, NC) as c:
                pool.wait_ge(normed, c)
                pool.dma_start(rows[:, :, :], x_chunks[c]).then_inc(rows_moved, 16)
            with pool.Fori(0, NC) as c:
                pool.wait_ge(normed, c + NC + 1)
                pool.dma_start(out_chunks[c], rows[:, :, :]).then_inc(rows_moved, 16)
            pool.wait_ge(rows_moved, 32 * NC)

        @block.scalar
        def _(act):
            def split_features(phase, J, B, dual, half):
                ops = operands(phase, dual)
                if not is_first(B):
                    act.wait_ge(unit_done, UNITS * B - UNITS + 2 * half + 2)
                if dual:
                    act.wait_ge(released, J + 2)
                elif phase == 1:
                    act.wait_ge(xw_ready, NC)
                elif phase == 2:
                    act.wait_ge(released, J + 2)
                else:
                    act.wait_ge(normed, J + 1)
                act.activation(w_hi[:, half, ops, :],
                               features[:, ops, bass.ds(J * CHUNK + half * HB, HB)], ACT.Copy).then_inc(w_hi_ready, 1)

            def split(phase, I, J, B, par, dual, hooks):
                for u in range(UNITS):
                    act.wait_ge(raw_loaded[u], 16 * B + 16)
                    if not is_first(B):
                        act.wait_ge(unit_done, UNITS * B - UNITS + u + 1)
                    if phase == 1:
                        for k in range(PAIR):
                            part = slice(k * CHUNK, (k + 1) * CHUNK)
                            at = bass.ds(J * TILES + PAIR * u + k, 1)
                            done = act.activation(hi[:, u, part], raw[:, u, part], ACT.Copy,
                                                  accum_out=deg_parts[:, I, at])
                        done.then_inc(hi_ready, 1)
                    else:
                        act.activation(hi[:, u, :], raw[:, u, :], ACT.Copy).then_inc(hi_ready, 1)
                    if u % 2 == 0:
                        split_features(phase, J, B, dual, u // 2)
                    if u in hooks:
                        hooks[u]()

            def epilogue(kind, chunk, m, par):
                def copy_out():
                    if kind == 1:
                        act.wait_ge(unit_done, UNITS * NC * (m + 1))
                    else:
                        act.wait_ge(unit_done, UNITS * first_block(3, m - 2 * NC + 1))
                    act.wait_ge(turned, m + 1)
                    if kind == 1:
                        act.activation(partial[:, bass.ds(chunk * CHUNK, CHUNK)],
                                       side[par][:, :, :].rearrange("p h n -> p (h n)"), ACT.Copy)
                    act.activation(turn[:, :], main[par][:, :, :].rearrange("p h n -> p (h n)"),
                                   ACT.Copy).then_inc(turn_ready, 1)

                def deviation():
                    act.wait_ge(var_ready, m - NC + 1)
                    act.activation(std[:, :], var[:, :], ACT.Sqrt, bias=eps_sb[:, :]).then_inc(std_ready, 1)

                if kind == 1:
                    return {3: copy_out}, {}
                if kind == 2:
                    return {}, {2: deviation}
                return {3: copy_out}, {2: deviation}

            act.wait_ge(consts_ready, 6)
            for c in range(NC):
                act.wait_ge(xw_summed, c + 1)
                banks = (main[1], side[1])[c % 2]
                act.activation(features[:, 0, c * CHUNK:(c + 1) * CHUNK],
                               banks[:, :, :].rearrange("p h n -> p (h n)"), ACT.Copy).then_inc(xw_ready, 1)
            act.wait_ge(xw_ready, NC)
            act.sem_inc(released, 1)
            act.wait_ge(side_zeroed, 1)
            walk(act, split, epilogue)

        @block.vector
        def _(dve):
            def split_features(phase, J, B, dual, half):
                ops = operands(phase, dual)
                dve.wait_ge(w_hi_ready, 2 * B + half + 1)
                dve.tensor_tensor(w_lo[:, half, ops, :],
                                  features[:, ops, bass.ds(J * CHUNK + half * HB, HB)],
                                  w_hi[:, half, ops, :].bitcast(F32), ALU.subtract).then_inc(w_lo_ready, 1)

            def split(phase, I, J, B, par, dual, hooks):
                for u in range(UNITS):
                    if u % 2 == 0:
                        split_features(phase, J, B, dual, u // 2)
                    dve.wait_ge(hi_ready, UNITS * B + u + 1)
                    if not (is_first(B) and u < LO_RING):
                        dve.wait_ge(unit_done, UNITS * B + u + 1 - LO_RING)
                    dve.tensor_tensor(lo[:, u % LO_RING, :], raw[:, u, :], hi[:, u, :].bitcast(F32),
                                      ALU.subtract).then_inc(lo_ready, 1)
                    if u in hooks:
                        hooks[u]()

            def invert_degrees():
                deg = inv_deg[:, :]
                dve.tensor_reduce(deg, deg_parts[:, :, :].rearrange("p c t -> p t c"), AX.X,
                                  ALU.add).then_inc(deg_step, 1)
                dve.wait_ge(deg_step, 1)
                dve.scalar_tensor_tensor(out=abs_deg[:, :], in0=deg, scalar=-1.0, in1=deg, op0=ALU.mult,
                                         op1=ALU.max).then_inc(deg_step, 1)
                dve.wait_ge(deg_step, 2)
                dve.tensor_scalar(no_inv[:, :], abs_deg[:, :], LARGEST_WITHOUT_INVERSE, None,
                                  ALU.is_le).then_inc(deg_step, 1)
                dve.wait_ge(deg_step, 3)
                dve.copy_predicated(deg, no_inv[:, :], ones[:, :]).then_inc(deg_step, 1)
                dve.wait_ge(deg_step, 4)
                dve.reciprocal(inv_deg[:, :], deg).then_inc(deg_step, 1)
                dve.wait_ge(deg_step, 5)
                dve.copy_predicated(inv_deg[:, :], no_inv[:, :], zero_col[:, :]).then_inc(deg_step, 1)
                dve.wait_ge(deg_step, 6)

            norm_steps = 9

            def epilogue(kind, chunk, m, par):
                turned_rows = main[par][:, :, :].rearrange("p h (t f) -> p (h t) f", f=P)
                tiles = bass.ds(chunk * TILES, TILES)
                columns = bass.ds(chunk * CHUNK, CHUNK)

                def per_row(column):
                    return column[:, tiles].unsqueeze(2).to_broadcast([P, TILES, P])

                def scale_rows():
                    dve.wait_ge(turned, m + 2)
                    dve.tensor_tensor(features[:, 1, columns].rearrange("p (t f) -> p t f", f=P),
                                      turned_rows, per_row(scale), ALU.mult).then_inc(released, 1)

                def add_parts():
                    dve.wait_ge(unit_done, UNITS * first_block(2, chunk + 1))
                    dve.wait_ge(turned, m + 1)
                    dve.scalar_tensor_tensor(out=turn[:, :], in0=main[par][:, :, :].rearrange("p h n -> p (h n)"),
                                             scalar=bias_sb[:, 0:1], in1=partial[:, columns],
                                             op0=ALU.add, op1=ALU.add).then_inc(turn_ready, 1)

                def moments_of_rows():
                    step = norm_steps * (m - NC)
                    dve.wait_ge(turned, m + 2)
                    if kind == 2:
                        dve.wait_ge(rows_moved, 16 * (chunk + 1))
                        dve.tensor_tensor(rows[:, :, :], turned_rows, rows[:, :, :], ALU.add)\
                           .then_inc(released, 1)
                    else:
                        dve.wait_ge(rows_moved, 16 * (NC + chunk))
                        dve.tensor_tensor(rows[:, :, :], turned_rows, per_row(inv_deg), ALU.mult)\
                           .then_inc(released, 1)
                    dve.wait_ge(released, m + 2)
                    if kind == 3:
                        dve.tensor_tensor(rows[:, :, :], rows[:, :, :],
                                          features[:, 0, columns].rearrange("p (t f) -> p t f", f=P),
                                          ALU.add).then_inc(norm_step, 1)
                    else:
                        dve.sem_inc(norm_step, 1)
                    dve.wait_ge(norm_step, step + 1)
                    for t in range(TILES):
                        done = dve.bn_stats(stats[:, t, :], rows[:, t, :])
                    done.then_inc(norm_step, 1)
                    dve.wait_ge(norm_step, step + 2)
                    even, odd = stats[:, :, 0:3], stats[:, :, 3:6]
                    dve.tensor_tensor(mean[:, :], even[:, :, 1], odd[:, :, 1], ALU.add)
                    dve.tensor_tensor(spread[:, :], even[:, :, 1], odd[:, :, 1], ALU.subtract)
                    dve.tensor_tensor(var[:, :], even[:, :, 2], odd[:, :, 2], ALU.add).then_inc(norm_step, 1)
                    dve.wait_ge(norm_step, step + 3)
                    dve.tensor_scalar(mean[:, :], mean[:, :], 0.5, None, ALU.mult)
                    dve.scalar_tensor_tensor(out=spread[:, :], in0=spread[:, :], scalar=0.25, in1=spread[:, :],
                                             op0=ALU.mult, op1=ALU.mult).then_inc(norm_step, 1)
                    dve.wait_ge(norm_step, step + 4)
                    dve.scalar_tensor_tensor(out=var[:, :], in0=var[:, :], scalar=1.0 / P, in1=spread[:, :],
                                             op0=ALU.mult, op1=ALU.add).then_inc(var_ready, 1)

                def norm_rows():
                    step = norm_steps * (m - NC)
                    dve.wait_ge(std_ready, m - NC + 1)
                    dve.wait_ge(var_ready, m - NC + 1)
                    dve.reciprocal(rstd[:, :], std[:, :]).then_inc(norm_step, 1)
                    dve.wait_ge(norm_step, step + 5)
                    dve.tensor_tensor(newton[:, :], rstd[:, :], rstd[:, :], ALU.mult).then_inc(norm_step, 1)
                    dve.wait_ge(norm_step, step + 6)
                    dve.scalar_tensor_tensor(out=newton[:, :], in0=var[:, :], scalar=EPS, in1=newton[:, :],
                                             op0=ALU.add, op1=ALU.mult).then_inc(norm_step, 1)
                    dve.wait_ge(norm_step, step + 7)
                    dve.tensor_scalar(newton[:, :], newton[:, :], -0.5, 1.5, ALU.mult, ALU.add).then_inc(norm_step, 1)
                    dve.wait_ge(norm_step, step + 8)
                    dve.tensor_tensor(rstd[:, :], rstd[:, :], newton[:, :], ALU.mult).then_inc(norm_step, 1)
                    dve.wait_ge(norm_step, step + 9)
                    for t in range(TILES):
                        if kind == 2:
                            to = features[:, 0, bass.ds(chunk * CHUNK + t * P, P)]
                        else:
                            to = rows[:, t, :]
                        done = dve.tensor_scalar(to, rows[:, t, :], mean[:, t:t + 1], rstd[:, t:t + 1],
                                                 ALU.subtract, ALU.mult)
                    done.then_inc(normed, 1)
                    if kind == 2 and isinstance(chunk, int) and chunk == NC - 1:
                        invert_degrees()

                if kind == 1:
                    return {3: scale_rows}, {}
                if kind == 2:
                    return {1: add_parts, 3: moments_of_rows}, {3: norm_rows}
                return {3: moments_of_rows}, {3: norm_rows}

            dve.memset(side[0][:, :, :], 0.0).then_inc(side_zeroed, 1)
            dve.wait_ge(small_loaded, 48)
            dve.tensor_tensor(filt_sb[:, :, :], d_sb[:, :, :], filt_sb[:, :, :], ALU.mult).then_inc(scale_step, 1)
            dve.wait_ge(scale_step, 1)
            dve.tensor_tensor(filt_sb[:, :, :], filt_sb[:, :, :], d_sb[:, :, :], ALU.mult).then_inc(scale_step, 1)
            dve.wait_ge(scale_step, 2)
            dve.tensor_tensor(scale[:, :], filt_sb[:, 0, :], filt_sb[:, 1, :], ALU.add).then_inc(scale_step, 1)
            for r in range(2, NR):
                dve.wait_ge(scale_step, r + 1)
                dve.tensor_tensor(scale[:, :], scale[:, :], filt_sb[:, r, :], ALU.add).then_inc(scale_step, 1)
            dve.wait_ge(scale_step, NR + 1)
            dve.wait_ge(consts_ready, 6)
            walk(dve, split, epilogue)

        @block.tensor
        def _(pe):
            def multiply(phase, I, J, B, par, dual, hooks):
                into = (main[par], side[par])
                for u in range(UNITS):
                    half, base = u // 2, (u % 2) * PAIR * P
                    weights = [[w[:, half, op, base + k * P:base + (k + 1) * P] for k in range(PAIR)]
                               for w in (w_hi, w_lo) for op in range(2)]
                    start = u == 0 and hooks is not None and "start" in hooks

                    def add(tile, w, first):
                        for n, op in enumerate((0, 1) if dual else (1,) if phase == 2 else (0,)):
                            for k in range(PAIR):
                                for b in range(HALVES):
                                    done = pe.matmul(into[n][:, b, :], weights[2 * w + op][k],
                                                     tile[:, k * CHUNK + b * BANK:k * CHUNK + (b + 1) * BANK],
                                                     start=first and k == 0, stop=False, skip_group_check=True)
                        return done

                    if u % 2 == 0:
                        pe.wait_ge(w_lo_ready, 2 * B + half + 1)
                    pe.wait_ge(hi_ready, UNITS * B + u + 1)
                    add(hi[:, u, :], 0, start)
                    add(hi[:, u, :], 1, False)
                    pe.wait_ge(lo_ready, UNITS * B + u + 1)
                    add(lo[:, u % LO_RING, :], 0, False).then_inc(unit_done, 1)
                    if hooks and u in hooks:
                        hooks[u]()

            def work(phase, I, J, B, par, dual, hooks):
                first = (phase == 3 and isinstance(J, int) and J == 0) or (phase < 3 and J is I)
                if first:
                    n = NC * (phase - 1) + I
                    if not is_first(n):
                        pe.wait_ge(released, n)
                    if phase == 1 and not (isinstance(I, int) and I == 0):
                        for b in range(HALVES):
                            pe.matmul(side[par][:, b, :], zeros[:, 0:P], zeros[:, :], start=True, stop=False,
                                      skip_group_check=True)
                    hooks = {**hooks, "start": True}
                multiply(phase, I, J, B, par, dual, hooks)

            def epilogue(kind, chunk, m, par):
                def transpose():
                    pe.wait_ge(turn_ready, m + 1)
                    for h in range(HALVES):
                        for t in range(BANK // P):
                            done = pe.transpose(main[par][:, h, t * P:(t + 1) * P],
                                                turn[:, h * BANK + t * P:h * BANK + (t + 1) * P], ident[:, :])
                    done.then_inc(turned, 1)

                return {2: transpose}, {}

            pe.wait_ge(w_loaded, 16)
            pe.wait_ge(consts_ready, 6)
            for c in range(NC):
                pe.wait_ge(xt_loaded[c], 16)
                if c >= 2:
                    pe.wait_ge(xw_ready, c - 1)
                banks = (main[1], side[1])[c % 2]
                for t in range(TILES):
                    done = pe.matmul(banks[:, t * P // BANK, t * P % BANK:t * P % BANK + P],
                                     partial[:, c * CHUNK + t * P:c * CHUNK + (t + 1) * P], w_sb[:, :],
                                     start=True, stop=True, skip_group_check=True)
                done.then_inc(xw_summed, 1)
            pe.sem_inc(turned, 1)
            walk(pe, work, epilogue)


def kernel(x, adj, L0_gnn_d_list, L0_gnn_weight, L0_gnn_filt, L0_gnn_bias):
    import numpy as np
    import concourse.bacc as bacc
    from concourse.bass_utils import run_bass_kernel_spmd

    def by_row_tile(a):
        a = np.asarray(a)
        return np.ascontiguousarray(a.reshape(a.shape[0], -1, P).transpose(2, 0, 1))

    x, adj, bias = np.asarray(x), np.asarray(adj), np.asarray(L0_gnn_bias)
    arrays = {
        "x": np.ascontiguousarray(x),
        "xT": np.ascontiguousarray(x.T),
        "A": np.ascontiguousarray(adj),
        "AT": np.ascontiguousarray(adj.T),
        "d": by_row_tile(L0_gnn_d_list),
        "filt": by_row_tile(L0_gnn_filt),
        "weight": np.ascontiguousarray(np.asarray(L0_gnn_weight)),
        "bias": np.ascontiguousarray(bias.reshape(P, 1)),
    }
    nc = bacc.Bacc("TRN2", target_bir_lowering=False, num_devices=1)
    args = [nc.dram_tensor(name, a.shape, F32, kind="ExternalInput").ap() for name, a in arrays.items()]
    out = nc.dram_tensor("out", x.shape, F32, kind="ExternalOutput").ap()
    build(nc, *args, out)
    r = run_bass_kernel_spmd(nc, [arrays], core_ids=[0])
    return r.results[0]["out"]
```

```python
from contextlib import ExitStack

import concourse.bass as bass
from concourse import mybir

F32 = mybir.dt.float32
F32R = mybir.dt.float32r
BF16 = mybir.dt.bfloat16
U32 = mybir.dt.uint32
ALU = mybir.AluOpType
ACT = mybir.ActivationFunctionType
AX = mybir.AxisListType

P = 128
CHUNK = 1024
BANK = 512
HALVES = CHUNK // BANK
TILES = CHUNK // P
PAIR = 1
UNITS = TILES // PAIR
UNIT = PAIR * CHUNK
HALF = UNITS // 2
QUARTER = UNITS // 4
LO_RING = UNITS // 2
EPS = 1e-5
LARGEST_WITHOUT_INVERSE = 2.0 ** -128


def build(nc, x, A, AT, d, filt, weight, bias, out):
    N = x.shape[0]
    NC = N // CHUNK
    T = N // P
    NR = d.shape[1]
    assert NC % 2 == 0 and NC >= 6

    A_units = A.rearrange("(j u two p) i -> j u p two i", u=UNITS, two=PAIR, p=P)
    AT_units = AT.rearrange("(j u two p) i -> j u p two i", u=UNITS, two=PAIR, p=P)
    x_chunks = x.rearrange("(c t p) f -> c p t f", t=TILES, p=P)
    out_chunks = out.rearrange("(c t p) f -> c p t f", t=TILES, p=P)

    def first_block3(I):
        return NC * NC + NC * (NC + 1) // 2 + NC * I

    with ExitStack() as ctx:
        def sb(name, shape, dt=F32):
            return ctx.enter_context(nc.sbuf_tensor(name, shape, dt))

        def sem(name):
            return ctx.enter_context(nc.semaphore(name))

        features = sb("features", [P, 2, N])
        partial = sb("partial", [P, N])
        raw = sb("raw", [P, UNITS, UNIT])
        assert N >= UNITS * UNIT
        slots = [raw[:, :, :], partial[:, 0:UNITS * UNIT].rearrange("p (u n) -> p u n", u=UNITS)]
        hi = sb("hi", [P, UNITS, UNIT], F32R)
        lo = sb("lo", [P, LO_RING, UNIT], F32R)
        HB = TILES // 2 * P
        w_hi = sb("w_hi", [P, 2, 2, HB], F32R)
        w_lo = sb("w_lo", [P, 2, 2, HB], F32R)
        turn = sb("turn", [P, CHUNK])
        rows = sb("rows", [P, TILES, P])
        deg_parts = sb("deg_parts", [P, NC, T])
        inv_deg = sb("inv_deg", [P, T])
        no_inv = sb("no_inv", [P, T], U32)
        zero_col = sb("zero_col", [P, T])
        ones = sb("ones", [P, T])
        abs_deg = sb("abs_deg", [P, T])
        d_sb = sb("d_sb", [P, NR, T])
        filt_sb = sb("filt_sb", [P, NR, T])
        scale = sb("scale", [P, T])
        w_sb = sb("w_sb", [P, P])
        bias_sb = sb("bias_sb", [P, 1])
        ident = sb("ident", [P, P])
        zeros = sb("zeros", [P, BANK], BF16)
        stats = sb("stats", [P, TILES, 6])
        mean2 = sb("mean2", [P, TILES])
        spread = sb("spread", [P, TILES])
        var4 = sb("var4", [P, TILES])
        rstd = sb("rstd", [P, TILES])
        half_rstd = sb("half_rstd", [P, TILES])
        minus_half = sb("minus_half", [P, TILES])
        shift = sb("shift", [P, TILES])
        main = [ctx.enter_context(nc.psum_tensor(f"main{p}", [P, HALVES, BANK], F32)) for p in range(2)]
        side = [ctx.enter_context(nc.psum_tensor(f"side{p}", [P, HALVES, BANK], F32)) for p in range(2)]
        main.append(side[0])

        x_loaded = [sem(f"x_loaded{c}") for c in range(NC)]
        small_loaded = sem("small_loaded")
        w_loaded = sem("w_loaded")
        consts_ready = sem("consts_ready")
        CONSTS = 6
        x_turned = sem("x_turned")
        x_turn_ready = sem("x_turn_ready")
        xw_summed = sem("xw_summed")
        xw_ready = sem("xw_ready")
        side_zeroed = sem("side_zeroed")
        scale_step = sem("scale_step")
        raw_loaded = [[sem(f"raw_loaded{s}_{u}") for u in range(UNITS)] for s in range(2)]
        hi_ready = sem("hi_ready")
        lo_ready = sem("lo_ready")
        unit_done = sem("unit_done")
        w_hi_ready = sem("w_hi_ready")
        w_lo_ready = sem("w_lo_ready")
        turn_ready = sem("turn_ready")
        turned = sem("turned")
        released = sem("released")
        stored = sem("stored")
        rows_free = sem("rows_free")
        residual_added = sem("residual_added")
        stats_ready = sem("stats_ready")
        factor_step = sem("factor_step")
        norm_ready = sem("norm_ready")
        scaled = sem("scaled")
        normed = sem("normed")
        deg_step = sem("deg_step")

        block = ctx.enter_context(nc.Block())

        x_turned_bank = side[1][:, :, :].rearrange("p h n -> p (h n)")
        xw_bank = main[1][:, :, :].rearrange("p h n -> p (h n)")

        XW_AHEAD = 2

        def walk(eng, work, epilogue, xw=None):

            def chunk1(I):
                par, B = I % 2, NC * I

                def single(J, B, hooks={}):
                    work(1, I, J, B, par, False, hooks)

                def dual(J, B):
                    work(1, I, J, B, par, True, {})

                lead = 3 if I == 1 else 1
                for k in range(lead):
                    single(I + k, B + k, epilogue(1, I - 1, I - 1, 1 - par, B)[0] if k == 0 else {})
                pairs = min(NC - I - lead, I)
                with eng.Fori(0, pairs) as k:
                    dual(k, B + lead + 2 * k)
                    single(I + lead + k, B + lead + 1 + 2 * k)
                if I + lead + pairs < NC:
                    with eng.Fori(I + lead + pairs, NC) as J:
                        single(J, B - I + pairs + J)
                if pairs < I:
                    with eng.Fori(pairs, I) as J:
                        dual(J, B + NC - I + J)

            def last_chunk1():
                B = NC * (NC - 1)
                work(1, NC - 1, NC - 1, B, 1, False, epilogue(1, NC - 2, NC - 2, 0, B)[0])
                work(1, NC - 1, 0, B + 1, 1, True, {})
                work(1, NC - 1, 1, B + 2, 1, True, {})

                def three(k):
                    work(1, NC - 1, 2 + k, B + 3 + 3 * k, 1, True, {})
                    work(2, 0, k, B + 4 + 3 * k, 0, False, {})
                    work(2, 1, 1 + k, B + 5 + 3 * k, 2, False, {})

                three(0)
                with eng.Fori(1, NC - 3) as k:
                    three(k)
                return B + 3 * (NC - 2)

            for J in range(NC):
                c = J + XW_AHEAD - (eng is nc.scalar)
                work(1, 0, J, J, 0, False, xw(c) if xw and XW_AHEAD <= c < NC else {})
            for I in range(1, NC - 1):
                chunk1(I)
            B = last_chunk1()

            kind, chunk, left = 1, NC - 1, 1
            for I in range(NC):
                acc = 2 if I == 1 else I % 2
                hooks = epilogue(kind, chunk, NC + I - 1, left, B)
                first_J = I + (NC - 3 if I < 2 else 0)
                peeled = min(NC - first_J, 2)
                for k in range(peeled):
                    work(2, I, first_J + k, B + k, acc, False, hooks[k])
                if first_J + peeled < NC:
                    with eng.Fori(first_J + peeled, NC) as J:
                        work(2, I, J, B - first_J + J, acc, False, {})
                B += NC - first_J
                kind, chunk, left = 2, I, acc

            def chunk3(I, par, kind):
                B = first_block3(I)
                hooks = epilogue(kind, I - 1 if kind == 3 else NC - 1, 2 * NC + I - 1, 1 - par, B)

                def pair(k, even_hooks, odd_hooks):
                    n, F = NC // 2 * I + k, first_block3(0)
                    even, odd = (0, F + n + 1, 2), (1, n - 1, 2)
                    if isinstance(n, int) and n < 2:
                        even = (0, F + 2 * n, 1)
                        odd = (0, F + 1, 1) if n == 0 else (1, 0, 0)
                    work(3, I, 2 * k, B + 2 * k, par, False, even_hooks, even)
                    work(3, I, 2 * k + 1, B + 2 * k + 1, par, False, odd_hooks, odd)

                pair(0, hooks[0], hooks[1])
                pair(1, hooks[2], {})
                with eng.Fori(2, NC // 2) as k:
                    pair(k, {}, {})

            chunk3(0, 0, 2)
            with eng.Fori(0, NC // 2 - 1) as q:
                chunk3(2 * q + 1, 1, 3)
                chunk3(2 * q + 2, 0, 3)
            chunk3(NC - 1, 1, 3)
            for hooks in epilogue(3, NC - 1, 3 * NC - 1, 1, first_block3(NC)):
                for hook in hooks.values():
                    hook()

        def is_first(B):
            return isinstance(B, int) and B == 0

        def run_hook(hooks, u):
            if (u + 1) % QUARTER == 0 and u // QUARTER in hooks:
                hooks[u // QUARTER]()

        def operands(phase, dual):
            return slice(0, 2) if dual else slice(1, 2) if phase == 2 else slice(0, 1)

        @block.sync
        def _(sp):
            sp.dma_start(w_sb[:, :], weight).then_inc(w_loaded, 16)

            def load_x(c):
                sp.dma_start(partial[:, c * CHUNK:(c + 1) * CHUNK].rearrange("p (t f) -> p t f", f=P),
                             x_chunks[c]).then_inc(x_loaded[c], 16)

            for c in range(XW_AHEAD):
                load_x(c)

            def load(phase, I, J, B, acc, dual, hooks, slot=None):
                which, used, back = slot or (0, B, 1)
                units = A_units if phase == 3 else AT_units
                for u in range(UNITS):
                    if is_first(used) and which == 1:
                        sp.wait_ge(released, NC + ((u + 1) * UNIT - 1) // CHUNK + 2)
                    elif not is_first(B):
                        sp.wait_ge(lo_ready, UNITS * (B - back) + u + 1)
                    sp.dma_start(slots[which][:, u, :].rearrange("p (two i) -> p two i", two=PAIR),
                                 units[J, u, :, :, bass.ds(I * CHUNK, CHUNK)]).then_inc(raw_loaded[which][u], 16)
                    run_hook(hooks, u)

            walk(sp, load, lambda *chunk: ({}, {}, {}), lambda c: {3: lambda: load_x(c)})

        @block.gpsimd
        def _(pool):
            pool.memset(ident[:, :], 0.0).then_inc(consts_ready, 1)
            pool.wait_ge(consts_ready, 1)
            pool.affine_select(out=ident[:, :], in_=ident[:, :], compare_op=ALU.not_equal, fill=1.0,
                               base=0, pattern=[[-1, P]], channel_multiplier=1).then_inc(consts_ready, 1)
            pool.memset(zeros[:, :], 0.0).then_inc(consts_ready, 1)
            pool.memset(zero_col[:, :], 0.0).then_inc(consts_ready, 1)
            pool.memset(minus_half[:, :], -0.5).then_inc(consts_ready, 1)
            pool.memset(ones[:, :], 1.0).then_inc(consts_ready, 1)
            pool.wait_ge(consts_ready, CONSTS)

            def norm_factors(chunks):
                even, odd = stats[:, :, 0:3], stats[:, :, 3:6]
                step = 5 * chunks
                pool.wait_ge(stats_ready, 2 * chunks + 2)
                pool.tensor_tensor(var4[:, :], even[:, :, 2], odd[:, :, 2], ALU.add)
                pool.tensor_tensor(mean2[:, :], even[:, :, 1], odd[:, :, 1], ALU.add)
                pool.tensor_tensor(spread[:, :], even[:, :, 1], odd[:, :, 1], ALU.subtract).then_inc(factor_step, 1)
                pool.wait_ge(factor_step, step + 1)
                pool.tensor_tensor(spread[:, :], spread[:, :], spread[:, :], ALU.mult)
                pool.tensor_scalar(var4[:, :], var4[:, :], 4.0 / P, 4.0 * EPS, ALU.mult, ALU.add).then_inc(factor_step, 1)
                pool.wait_ge(factor_step, step + 2)
                pool.tensor_tensor(var4[:, :], var4[:, :], spread[:, :], ALU.add).then_inc(factor_step, 1)
                pool.wait_ge(factor_step, step + 3)
                pool.tensor_tensor(half_rstd[:, :], var4[:, :], minus_half[:, :], ALU.pow).then_inc(factor_step, 1)
                pool.wait_ge(factor_step, step + 4)
                pool.tensor_tensor(mean2[:, :], mean2[:, :], half_rstd[:, :], ALU.mult)
                pool.tensor_tensor(rstd[:, :], half_rstd[:, :], half_rstd[:, :], ALU.add).then_inc(factor_step, 1)
                pool.wait_ge(factor_step, step + 5)
                pool.tensor_tensor(shift[:, :], zero_col[:, 0:TILES], mean2[:, :], ALU.subtract).then_inc(norm_ready, 1)

            def norm(chunks, to):
                norm_factors(chunks)
                per_row = lambda column: column[:, :].unsqueeze(2).to_broadcast([P, TILES, P])
                pool.wait_ge(norm_ready, 2 * chunks + 1)
                pool.tensor_tensor(rows[:, :, :], rows[:, :, :], per_row(rstd), ALU.mult).then_inc(norm_ready, 1)
                pool.wait_ge(norm_ready, 2 * chunks + 2)
                pool.tensor_tensor(to, rows[:, :, :], per_row(shift), ALU.add).then_inc(normed, 1)

            with pool.Fori(0, NC) as c:
                norm(c, features[:, 0, bass.ds(c * CHUNK, CHUNK)].rearrange("p (t f) -> p t f", f=P))
            pool.wait_ge(normed, NC)
            pool.sem_inc(rows_free, 1)
            with pool.Fori(0, NC) as c:
                norm(c + NC, rows[:, :, :])
                pool.wait_ge(normed, c + NC + 1)
                pool.dma_start(out_chunks[c], rows[:, :, :]).then_inc(stored, 16)
                pool.wait_ge(stored, 16 * c + 16)
                pool.sem_inc(rows_free, 1)

        @block.scalar
        def _(act):
            def split_features(phase, I, J, B, dual, half):
                ops = operands(phase, dual)
                if not is_first(B):
                    act.wait_ge(unit_done, UNITS * B - UNITS + HALF * (half + 1))
                if dual:
                    act.wait_ge(scaled, J + 1)
                elif phase == 1:
                    act.wait_ge(xw_ready, J + 1 if is_first(I) else NC)
                elif phase == 2:
                    act.wait_ge(scaled, J + 1)
                else:
                    act.wait_ge(normed, J + 1)
                act.activation(w_hi[:, half, ops, :],
                               features[:, ops, bass.ds(J * CHUNK + half * HB, HB)], ACT.Copy).then_inc(w_hi_ready, 1)

            def split(phase, I, J, B, acc, dual, hooks, slot=None):
                which, used, _ = slot or (0, B, 1)
                for u in range(UNITS):
                    act.wait_ge(raw_loaded[which][u], 16 * used + 16)
                    if not is_first(B):
                        act.wait_ge(unit_done, UNITS * B - UNITS + u + 1)
                    if phase == 1:
                        for k in range(PAIR):
                            part = slice(k * CHUNK, (k + 1) * CHUNK)
                            at = bass.ds(J * TILES + PAIR * u + k, 1)
                            done = act.activation(hi[:, u, part], slots[which][:, u, part], ACT.Copy,
                                                  accum_out=deg_parts[:, I, at])
                        done.then_inc(hi_ready, 1)
                    else:
                        act.activation(hi[:, u, :], slots[which][:, u, :], ACT.Copy).then_inc(hi_ready, 1)
                    if u % HALF == 0:
                        split_features(phase, I, J, B, dual, u // HALF)
                    run_hook(hooks, u)

            def epilogue(kind, chunk, m, acc, done):
                def copy_out():
                    act.wait_ge(unit_done, UNITS * done)
                    summed = main[acc][:, :, :].rearrange("p h n -> p (h n)")
                    if kind == 1:
                        act.activation(rows[:, :, :], side[acc][:, :, :].rearrange("p h (t f) -> p (h t) f", f=P), ACT.Copy)
                    if kind == 2:
                        act.wait_ge(small_loaded, 48)
                        act.activation(turn[:, :], summed, ACT.Identity, bias=bias_sb[:, :]).then_inc(turn_ready, 1)
                    else:
                        act.activation(turn[:, :], summed, ACT.Copy).then_inc(turn_ready, 1)

                return {2: copy_out}, {}, {}

            act.dma_start(d_sb[:, :, :], d).then_inc(small_loaded, 16)
            act.dma_start(filt_sb[:, :, :], filt).then_inc(small_loaded, 16)
            act.dma_start(bias_sb[:, :], bias).then_inc(small_loaded, 16)

            def copy_xw(c):
                def copy_turned():
                    act.wait_ge(x_turned, c + 1)
                    act.activation(turn[:, :], x_turned_bank, ACT.Copy).then_inc(x_turn_ready, 1)

                def copy_product():
                    act.wait_ge(xw_summed, c + 1)
                    act.activation(features[:, 0, c * CHUNK:(c + 1) * CHUNK], xw_bank, ACT.Copy).then_inc(xw_ready, 1)
                    if c == NC - 1:
                        act.wait_ge(xw_ready, NC)
                        act.sem_inc(released, 1)

                return {1: copy_turned, 3: copy_product}

            for c in range(XW_AHEAD):
                for step in copy_xw(c).values():
                    step()
            act.wait_ge(side_zeroed, 1)
            walk(act, split, epilogue, copy_xw)

        @block.vector
        def _(dve):
            def split_features(phase, J, B, dual, half):
                ops = operands(phase, dual)
                dve.wait_ge(w_hi_ready, 2 * B + half + 1)
                dve.tensor_tensor(w_lo[:, half, ops, :],
                                  features[:, ops, bass.ds(J * CHUNK + half * HB, HB)],
                                  w_hi[:, half, ops, :].bitcast(F32), ALU.subtract).then_inc(w_lo_ready, 1)

            def split(phase, I, J, B, acc, dual, hooks, slot=None):
                which, used, _ = slot or (0, B, 1)
                for u in range(UNITS):
                    if u % HALF == 0:
                        split_features(phase, J, B, dual, u // HALF)
                    dve.wait_ge(hi_ready, UNITS * B + u + 1)
                    if not (is_first(B) and u < LO_RING):
                        dve.wait_ge(unit_done, UNITS * B + u + 1 - LO_RING)
                    dve.tensor_tensor(lo[:, u % LO_RING, :], slots[which][:, u, :], hi[:, u, :].bitcast(F32),
                                      ALU.subtract).then_inc(lo_ready, 1)
                    run_hook(hooks, u)

            def invert_degrees():
                deg = inv_deg[:, :]
                dve.tensor_reduce(deg, deg_parts[:, :, :].rearrange("p c t -> p t c"), AX.X,
                                  ALU.add).then_inc(deg_step, 1)
                dve.wait_ge(deg_step, 1)
                dve.scalar_tensor_tensor(out=abs_deg[:, :], in0=deg, scalar=-1.0, in1=deg, op0=ALU.mult,
                                         op1=ALU.max).then_inc(deg_step, 1)
                dve.wait_ge(deg_step, 2)
                dve.tensor_scalar(no_inv[:, :], abs_deg[:, :], LARGEST_WITHOUT_INVERSE, None,
                                  ALU.is_le).then_inc(deg_step, 1)
                dve.wait_ge(deg_step, 3)
                dve.copy_predicated(deg, no_inv[:, :], ones[:, :]).then_inc(deg_step, 1)
                dve.wait_ge(deg_step, 4)
                dve.reciprocal(inv_deg[:, :], deg).then_inc(deg_step, 1)
                dve.wait_ge(deg_step, 5)
                dve.copy_predicated(inv_deg[:, :], no_inv[:, :], zero_col[:, :]).then_inc(deg_step, 1)
                dve.wait_ge(deg_step, 6)

            def epilogue(kind, chunk, m, acc, done):
                def turned_rows(banks):
                    return banks[acc][:, :, :].rearrange("p h (t f) -> p (h t) f", f=P)

                tiles = bass.ds(chunk * TILES, TILES)
                columns = bass.ds(chunk * CHUNK, CHUNK)

                def per_row(column):
                    return column[:, tiles].unsqueeze(2).to_broadcast([P, TILES, P])

                def keep_rows():
                    dve.wait_ge(turned, m + 1)
                    dve.tensor_tensor(features[:, 1, columns].rearrange("p (t f) -> p t f", f=P),
                                      turned_rows(main), per_row(scale), ALU.mult).then_inc(scaled, 1)
                    kept = partial[:, columns].rearrange("p (t f) -> p t f", f=P)
                    dve.tensor_tensor(kept, turned_rows(side), kept, ALU.add).then_inc(released, 1)

                def add_up():
                    dve.wait_ge(turned, m + 1)
                    if kind == 2:
                        if chunk:
                            dve.wait_ge(normed, chunk)
                        dve.tensor_tensor(rows[:, :, :], turned_rows(main),
                                          partial[:, columns].rearrange("p (t f) -> p t f", f=P),
                                          ALU.add).then_inc(released, 1)
                    else:
                        dve.wait_ge(rows_free, chunk + 1)
                        dve.tensor_tensor(rows[:, :, :], turned_rows(main), per_row(inv_deg), ALU.mult)\
                           .then_inc(released, 1)

                def add_residual():
                    dve.wait_ge(released, m + 2)
                    dve.tensor_tensor(rows[:, :, :], rows[:, :, :],
                                      features[:, 0, columns].rearrange("p (t f) -> p t f", f=P),
                                      ALU.add).then_inc(residual_added, 1)

                def statistics(tiles):
                    if kind == 2:
                        dve.wait_ge(released, m + 2)
                    else:
                        dve.wait_ge(residual_added, chunk + 1)
                    for t in tiles:
                        done = dve.bn_stats(stats[:, t, :], rows[:, t, :])
                    done.then_inc(stats_ready, 1)

                first_half = lambda: statistics(range(TILES // 2))
                last_half = lambda: statistics(range(TILES // 2, TILES))
                if kind == 1:
                    return {3: keep_rows}, {}, {}
                if kind == 3:
                    return {3: add_up}, {1: add_residual, 3: first_half}, {1: last_half}
                if chunk == NC - 2:
                    return {3: lambda: (add_up(), first_half(), last_half())}, {}, {}
                return {3: add_up}, {0: first_half, 1: last_half}, {3: invert_degrees} if m == 2 * NC - 1 else {}

            dve.memset(side[0][:, :, :], 0.0).then_inc(side_zeroed, 1)
            dve.wait_ge(small_loaded, 48)
            dve.tensor_tensor(filt_sb[:, :, :], d_sb[:, :, :], filt_sb[:, :, :], ALU.mult).then_inc(scale_step, 1)
            dve.wait_ge(scale_step, 1)
            dve.tensor_tensor(filt_sb[:, :, :], filt_sb[:, :, :], d_sb[:, :, :], ALU.mult).then_inc(scale_step, 1)
            dve.wait_ge(scale_step, 2)
            dve.tensor_tensor(scale[:, :], filt_sb[:, 0, :], filt_sb[:, 1, :], ALU.add).then_inc(scale_step, 1)
            for r in range(2, NR):
                dve.wait_ge(scale_step, r + 1)
                dve.tensor_tensor(scale[:, :], scale[:, :], filt_sb[:, r, :], ALU.add).then_inc(scale_step, 1)
            dve.wait_ge(scale_step, NR + 1)
            dve.wait_ge(consts_ready, CONSTS)
            walk(dve, split, epilogue)

        @block.tensor
        def _(pe):
            def multiply(phase, J, B, acc, dual, hooks, first):
                into = (main[acc], side[acc] if dual else None)
                for u in range(UNITS):
                    half, base = u // HALF, (u % HALF) * PAIR * P
                    weights = [[w[:, half, op, base + k * P:base + (k + 1) * P] for k in range(PAIR)]
                               for w in (w_hi, w_lo) for op in range(2)]
                    start = first and u == 0

                    def add(tile, w, start):
                        for n, op in enumerate((0, 1) if dual else (1,) if phase == 2 else (0,)):
                            for k in range(PAIR):
                                for b in range(HALVES):
                                    done = pe.matmul(into[n][:, b, :], weights[2 * w + op][k],
                                                     tile[:, k * CHUNK + b * BANK:k * CHUNK + (b + 1) * BANK],
                                                     start=start and k == 0, stop=False, skip_group_check=True)
                        return done

                    if u % HALF == 0:
                        pe.wait_ge(w_lo_ready, 2 * B + half + 1)
                    pe.wait_ge(hi_ready, UNITS * B + u + 1)
                    add(hi[:, u, :], 0, start)
                    add(hi[:, u, :], 1, False)
                    pe.wait_ge(lo_ready, UNITS * B + u + 1)
                    add(lo[:, u % LO_RING, :], 0, False).then_inc(unit_done, 1)
                    run_hook(hooks, u)

            def work(phase, I, J, B, acc, dual, hooks, slot=None):
                first = isinstance(J, int) and J == (0 if phase == 3 else I)
                if first:
                    n = NC * (phase - 1) + (0 if phase == 2 and I == 1 else I)
                    if not is_first(n):
                        pe.wait_ge(released, n)
                    if phase == 1 and not (isinstance(I, int) and I == 0):
                        for b in range(HALVES):
                            pe.matmul(side[acc][:, b, :], zeros[:, 0:P], zeros[:, :], start=True, stop=False,
                                      skip_group_check=True)
                multiply(phase, J, B, acc, dual, hooks, first)

            def epilogue(kind, chunk, m, acc, done):
                def transpose():
                    pe.wait_ge(turn_ready, m + 1)
                    pairs = ((side, rows[:, :, :].rearrange("p t f -> p (t f)")),) if kind == 1 else ()
                    for banks, source in (*pairs, (main, turn[:, :])):
                        for h in range(HALVES):
                            for t in range(BANK // P):
                                done = pe.transpose(banks[acc][:, h, t * P:(t + 1) * P],
                                                    source[:, h * BANK + t * P:h * BANK + (t + 1) * P], ident[:, :])
                    done.then_inc(turned, 1)

                return {1: transpose}, {}, {}

            def multiply_xw(c):
                def turn_x():
                    pe.wait_ge(x_loaded[c], 16)
                    if c:
                        pe.wait_ge(x_turn_ready, c)
                    for t in range(TILES):
                        at = slice(t * P, (t + 1) * P)
                        done = pe.transpose(x_turned_bank[:, at], partial[:, c * CHUNK + t * P:c * CHUNK + (t + 1) * P],
                                            ident[:, :])
                    done.then_inc(x_turned, 1)

                def multiply_x():
                    pe.wait_ge(x_turn_ready, c + 1)
                    if c:
                        pe.wait_ge(xw_ready, c)
                    for t in range(TILES):
                        at = slice(t * P, (t + 1) * P)
                        done = pe.matmul(xw_bank[:, at], turn[:, at], w_sb[:, :], start=True, stop=True,
                                         skip_group_check=True)
                    done.then_inc(xw_summed, 1)

                return {1: turn_x, 3: multiply_x}

            pe.wait_ge(consts_ready, CONSTS)
            pe.wait_ge(w_loaded, 16)
            for c in range(XW_AHEAD):
                for step in multiply_xw(c).values():
                    step()
            walk(pe, work, epilogue, multiply_xw)


def kernel(x, adj, L0_gnn_d_list, L0_gnn_weight, L0_gnn_filt, L0_gnn_bias):
    import numpy as np
    import concourse.bacc as bacc
    from concourse.bass_utils import run_bass_kernel_spmd

    def by_row_tile(a):
        a = np.asarray(a)
        return np.ascontiguousarray(a.reshape(a.shape[0], -1, P).transpose(2, 0, 1))

    x, adj, bias = np.asarray(x), np.asarray(adj), np.asarray(L0_gnn_bias)
    arrays = {
        "x": np.ascontiguousarray(x),
        "A": np.ascontiguousarray(adj),
        "AT": np.ascontiguousarray(adj.T),
        "d": by_row_tile(L0_gnn_d_list),
        "filt": by_row_tile(L0_gnn_filt),
        "weight": np.ascontiguousarray(np.asarray(L0_gnn_weight)),
        "bias": np.ascontiguousarray(bias.reshape(P, 1)),
    }
    nc = bacc.Bacc("TRN2", target_bir_lowering=False, num_devices=1)
    args = [nc.dram_tensor(name, a.shape, F32, kind="ExternalInput").ap() for name, a in arrays.items()]
    out = nc.dram_tensor("out", x.shape, F32, kind="ExternalOutput").ap()
    build(nc, *args, out)
    r = run_bass_kernel_spmd(nc, [arrays], core_ids=[0])
    return r.results[0]["out"]
```

```python
from contextlib import ExitStack

import concourse.bass as bass
from concourse import mybir

F32 = mybir.dt.float32
F32R = mybir.dt.float32r
BF16 = mybir.dt.bfloat16
U32 = mybir.dt.uint32
ALU = mybir.AluOpType
ACT = mybir.ActivationFunctionType
AX = mybir.AxisListType

P = 128
CHUNK = 1024
BANK = 512
HALVES = CHUNK // BANK
TILES = CHUNK // P
UNIT_TILES = 1
UNITS = TILES // UNIT_TILES
UNIT = UNIT_TILES * CHUNK
HALF = UNITS // 2
QUARTER = UNITS // 4
LO_RING = UNITS // 2
EPS = 1e-5
LARGEST_WITHOUT_INVERSE = 2.0 ** -128


def build(nc, x, A, AT, d, filt, weight, bias, out):
    N = x.shape[0]
    NC = N // CHUNK
    T = N // P
    NR = d.shape[1]
    assert NC % 2 == 0 and NC >= 8

    A_units = A.rearrange("(j u k p) i -> j u p k i", u=UNITS, k=UNIT_TILES, p=P)
    AT_units = AT.rearrange("(j u k p) i -> j u p k i", u=UNITS, k=UNIT_TILES, p=P)
    x_chunks = x.rearrange("(c t p) f -> c p t f", t=TILES, p=P)
    out_chunks = out.rearrange("(c t p) f -> c p t f", t=TILES, p=P)

    def first_block3(I):
        return NC * NC + NC * (NC + 1) // 2 + NC * I

    with ExitStack() as ctx:
        def sb(name, shape, dt=F32):
            return ctx.enter_context(nc.sbuf_tensor(name, shape, dt))

        def sem(name):
            return ctx.enter_context(nc.semaphore(name))

        features = sb("features", [P, 2, N])
        partial = sb("partial", [P, N])
        raw = sb("raw", [P, UNITS, UNIT])
        assert N >= UNITS * UNIT
        slots = [raw[:, :, :], partial[:, 0:UNITS * UNIT].rearrange("p (u n) -> p u n", u=UNITS)]
        hi = sb("hi", [P, UNITS, UNIT], F32R)
        lo = sb("lo", [P, LO_RING, UNIT], F32R)
        HB = TILES // 2 * P
        w_hi = sb("w_hi", [P, 2, 2, HB], F32R)
        w_lo = sb("w_lo", [P, 2, 2, HB], F32R)
        turn = sb("turn", [P, CHUNK])
        rows = sb("rows", [P, TILES, P])
        deg_parts = sb("deg_parts", [P, NC, T])
        inv_deg = sb("inv_deg", [P, T])
        no_inv = sb("no_inv", [P, T], U32)
        zero_col = sb("zero_col", [P, T])
        ones = sb("ones", [P, T])
        abs_deg = sb("abs_deg", [P, T])
        d_sb = sb("d_sb", [P, NR, T])
        filt_sb = sb("filt_sb", [P, NR, T])
        scale = sb("scale", [P, T])
        w_sb = sb("w_sb", [P, P])
        bias_sb = sb("bias_sb", [P, 1])
        ident = sb("ident", [P, P])
        zeros = sb("zeros", [P, BANK], BF16)
        stats = sb("stats", [P, TILES, 6])
        mean2 = sb("mean2", [P, TILES])
        spread = sb("spread", [P, TILES])
        var4 = sb("var4", [P, TILES])
        rstd = sb("rstd", [P, TILES])
        half_rstd = sb("half_rstd", [P, TILES])
        minus_half = sb("minus_half", [P, TILES])
        shift = sb("shift", [P, TILES])
        main = [ctx.enter_context(nc.psum_tensor(f"main{p}", [P, HALVES, BANK], F32)) for p in range(2)]
        side = [ctx.enter_context(nc.psum_tensor(f"side{p}", [P, HALVES, BANK], F32)) for p in range(2)]
        main.append(side[0])

        x_loaded = [sem(f"x_loaded{c}") for c in range(NC)]
        small_loaded = sem("small_loaded")
        w_loaded = sem("w_loaded")
        consts_ready = sem("consts_ready")
        CONSTS = 6
        x_turned = sem("x_turned")
        x_turn_ready = sem("x_turn_ready")
        xw_summed = sem("xw_summed")
        xw_ready = sem("xw_ready")
        side_zeroed = sem("side_zeroed")
        scale_step = sem("scale_step")
        raw_loaded = [[sem(f"raw_loaded{s}_{u}") for u in range(UNITS)] for s in range(2)]
        hi_ready = sem("hi_ready")
        lo_ready = sem("lo_ready")
        unit_done = sem("unit_done")
        w_hi_ready = sem("w_hi_ready")
        w_lo_ready = sem("w_lo_ready")
        turn_ready = sem("turn_ready")
        turned = sem("turned")
        released = sem("released")
        stored = sem("stored")
        rows_free = sem("rows_free")
        residual_added = sem("residual_added")
        stats_ready = sem("stats_ready")
        factor_step = sem("factor_step")
        norm_ready = sem("norm_ready")
        scaled = sem("scaled")
        normed = sem("normed")
        deg_step = sem("deg_step")

        block = ctx.enter_context(nc.Block())

        x_turned_bank = side[1][:, :, :].rearrange("p h n -> p (h n)")
        xw_bank = main[1][:, :, :].rearrange("p h n -> p (h n)")

        XW_AHEAD = 2

        def walk(eng, work, epilogue, xw=None):

            def chunk1(I):
                par, B = I % 2, NC * I

                def single(J, B, hooks={}):
                    work(1, I, J, B, par, False, hooks)

                def dual(J, B):
                    work(1, I, J, B, par, True, {})

                lead = 3 if I == 1 else 1
                for k in range(lead):
                    single(I + k, B + k, epilogue(1, I - 1, I - 1, 1 - par, B)[0] if k == 0 else {})
                pairs = min(NC - I - lead, I)
                with eng.Fori(0, pairs) as k:
                    dual(k, B + lead + 2 * k)
                    single(I + lead + k, B + lead + 1 + 2 * k)
                if I + lead + pairs < NC:
                    with eng.Fori(I + lead + pairs, NC) as J:
                        single(J, B - I + pairs + J)
                if pairs < I:
                    with eng.Fori(pairs, I) as J:
                        dual(J, B + NC - I + J)

            def last_chunk1():
                B = NC * (NC - 1)
                work(1, NC - 1, NC - 1, B, 1, False, epilogue(1, NC - 2, NC - 2, 0, B)[0])
                work(1, NC - 1, 0, B + 1, 1, True, {})
                work(1, NC - 1, 1, B + 2, 1, True, {})

                def three(k):
                    work(1, NC - 1, 2 + k, B + 3 + 3 * k, 1, True, {})
                    work(2, 0, k, B + 4 + 3 * k, 0, False, {})
                    work(2, 1, 1 + k, B + 5 + 3 * k, 2, False, {})

                three(0)
                with eng.Fori(1, NC - 3) as k:
                    three(k)
                return B + 3 * (NC - 2)

            for J in range(NC):
                work(1, 0, J, J, 0, False, xw(J) if xw else {})
            for I in range(1, NC - 1):
                chunk1(I)
            B = last_chunk1()

            kind, chunk, left = 1, NC - 1, 1
            late = {}
            for I in range(NC):
                acc = 2 if I == 1 else I % 2
                hooks = epilogue(kind, chunk, NC + I - 1, left, B)
                first_J = I + (NC - 3 if I < 2 else 0)
                peeled = min(NC - first_J, 3)
                left_over = {u: hook for group in hooks[peeled:3] for u, hook in group.items()}
                for k in range(peeled):
                    work(2, I, first_J + k, B + k, acc, False, {**late, **hooks[k]})
                    late = {}
                if first_J + peeled < NC:
                    with eng.Fori(first_J + peeled, NC) as J:
                        work(2, I, J, B - first_J + J, acc, False, {})
                B += NC - first_J
                kind, chunk, left, late = 2, I, acc, left_over

            def chunk3(I, par, kind, late={}):
                B = first_block3(I)
                hooks = epilogue(kind, I - 1 if kind == 3 else NC - 1, 2 * NC + I - 1, 1 - par, B)

                def pair(k, even_hooks, odd_hooks):
                    n, F = NC // 2 * I + k, first_block3(0)
                    even, odd = (0, F + n + 1, 2), (1, n - 1, 2)
                    if isinstance(n, int) and n < 2:
                        even = (0, F + 2 * n, 1)
                        odd = (0, F + 1, 1) if n == 0 else (1, 0, 0)
                    work(3, I, 2 * k, B + 2 * k, par, False, even_hooks, even)
                    work(3, I, 2 * k + 1, B + 2 * k + 1, par, False, odd_hooks, odd)

                pair(0, {**late, **hooks[0]}, hooks[1])
                pair(1, hooks[2], hooks[3])
                with eng.Fori(2, NC // 2) as k:
                    pair(k, {}, {})

            chunk3(0, 0, 2, late)
            with eng.Fori(0, NC // 2 - 1) as q:
                chunk3(2 * q + 1, 1, 3)
                chunk3(2 * q + 2, 0, 3)
            chunk3(NC - 1, 1, 3)
            for hooks in epilogue(3, NC - 1, 3 * NC - 1, 1, first_block3(NC)):
                for hook in hooks.values():
                    hook()

        def is_first(B):
            return isinstance(B, int) and B == 0

        def run_hook(hooks, u):
            if (u + 1) % QUARTER == 0 and u // QUARTER in hooks:
                hooks[u // QUARTER]()

        def operands(phase, dual):
            return slice(0, 2) if dual else slice(1, 2) if phase == 2 else slice(0, 1)

        @block.sync
        def _(sp):
            sp.dma_start(w_sb[:, :], weight).then_inc(w_loaded, 16)

            def load_x(c):
                sp.dma_start(partial[:, c * CHUNK:(c + 1) * CHUNK].rearrange("p (t f) -> p t f", f=P),
                             x_chunks[c]).then_inc(x_loaded[c], 16)

            for c in range(XW_AHEAD):
                load_x(c)

            def load(phase, I, J, B, acc, dual, hooks, slot=None):
                which, used, back = slot or (0, B, 1)
                units = A_units if phase == 3 else AT_units
                for u in range(UNITS):
                    if is_first(used) and which == 1:
                        sp.wait_ge(released, NC + ((u + 1) * UNIT - 1) // CHUNK + 2)
                    elif not is_first(B):
                        sp.wait_ge(lo_ready, UNITS * (B - back) + u + 1)
                    sp.dma_start(slots[which][:, u, :].rearrange("p (k i) -> p k i", k=UNIT_TILES),
                                 units[J, u, :, :, bass.ds(I * CHUNK, CHUNK)]).then_inc(raw_loaded[which][u], 16)
                    run_hook(hooks, u)

            walk(sp, load, lambda *chunk: ({}, {}, {}, {}),
                 lambda J: {3: lambda: load_x(J + XW_AHEAD)} if J + XW_AHEAD < NC else {})

        @block.gpsimd
        def _(pool):
            pool.memset(ident[:, :], 0.0).then_inc(consts_ready, 1)
            pool.wait_ge(consts_ready, 1)
            pool.affine_select(out=ident[:, :], in_=ident[:, :], compare_op=ALU.not_equal, fill=1.0,
                               base=0, pattern=[[-1, P]], channel_multiplier=1).then_inc(consts_ready, 1)
            pool.memset(zeros[:, :], 0.0).then_inc(consts_ready, 1)
            pool.memset(zero_col[:, :], 0.0).then_inc(consts_ready, 1)
            pool.memset(minus_half[:, :], -0.5).then_inc(consts_ready, 1)
            pool.memset(ones[:, :], 1.0).then_inc(consts_ready, 1)
            pool.wait_ge(consts_ready, CONSTS)

            def norm_factors(chunks):
                even, odd = stats[:, :, 0:3], stats[:, :, 3:6]
                step = 5 * chunks
                pool.wait_ge(stats_ready, 2 * chunks + 2)
                pool.tensor_tensor(var4[:, :], even[:, :, 2], odd[:, :, 2], ALU.add)
                pool.tensor_tensor(mean2[:, :], even[:, :, 1], odd[:, :, 1], ALU.add)
                pool.tensor_tensor(spread[:, :], even[:, :, 1], odd[:, :, 1], ALU.subtract).then_inc(factor_step, 1)
                pool.wait_ge(factor_step, step + 1)
                pool.tensor_tensor(spread[:, :], spread[:, :], spread[:, :], ALU.mult)
                pool.tensor_scalar(var4[:, :], var4[:, :], 4.0 / P, 4.0 * EPS, ALU.mult, ALU.add).then_inc(factor_step, 1)
                pool.wait_ge(factor_step, step + 2)
                pool.tensor_tensor(var4[:, :], var4[:, :], spread[:, :], ALU.add).then_inc(factor_step, 1)
                pool.wait_ge(factor_step, step + 3)
                pool.tensor_tensor(half_rstd[:, :], var4[:, :], minus_half[:, :], ALU.pow).then_inc(factor_step, 1)
                pool.wait_ge(factor_step, step + 4)
                pool.tensor_tensor(mean2[:, :], mean2[:, :], half_rstd[:, :], ALU.mult)
                pool.tensor_tensor(rstd[:, :], half_rstd[:, :], half_rstd[:, :], ALU.add).then_inc(factor_step, 1)
                pool.wait_ge(factor_step, step + 5)
                pool.tensor_tensor(shift[:, :], zero_col[:, 0:TILES], mean2[:, :], ALU.subtract).then_inc(norm_ready, 1)

            with pool.Fori(0, NC) as c:
                norm_factors(c)
            pool.wait_ge(normed, 2 * NC)
            pool.sem_inc(rows_free, 1)
            with pool.Fori(0, NC) as c:
                norm_factors(c + NC)
                pool.wait_ge(normed, 2 * (c + NC) + 2)
                pool.dma_start(out_chunks[c], rows[:, :, :]).then_inc(stored, 16)
                pool.wait_ge(stored, 16 * c + 16)
                pool.sem_inc(rows_free, 1)

        @block.scalar
        def _(act):
            def split_features(phase, I, J, B, dual, half):
                ops = operands(phase, dual)
                if not is_first(B):
                    act.wait_ge(unit_done, UNITS * B - UNITS + HALF * (half + 1))
                if dual:
                    act.wait_ge(scaled, J + 1)
                elif phase == 1:
                    act.wait_ge(xw_ready, J + 1 if is_first(I) else NC)
                elif phase == 2:
                    act.wait_ge(scaled, J + 1)
                else:
                    act.wait_ge(normed, 2 * J + 2)
                act.activation(w_hi[:, half, ops, :],
                               features[:, ops, bass.ds(J * CHUNK + half * HB, HB)], ACT.Copy).then_inc(w_hi_ready, 1)

            def split(phase, I, J, B, acc, dual, hooks, slot=None):
                which, used, _ = slot or (0, B, 1)
                for u in range(UNITS):
                    act.wait_ge(raw_loaded[which][u], 16 * used + 16)
                    if not is_first(B):
                        act.wait_ge(unit_done, UNITS * B - UNITS + u + 1)
                    if phase == 1:
                        for k in range(UNIT_TILES):
                            part = slice(k * CHUNK, (k + 1) * CHUNK)
                            at = bass.ds(J * TILES + UNIT_TILES * u + k, 1)
                            done = act.activation(hi[:, u, part], slots[which][:, u, part], ACT.Copy,
                                                  accum_out=deg_parts[:, I, at])
                        done.then_inc(hi_ready, 1)
                    else:
                        act.activation(hi[:, u, :], slots[which][:, u, :], ACT.Copy).then_inc(hi_ready, 1)
                    if u % HALF == 0:
                        split_features(phase, I, J, B, dual, u // HALF)
                    run_hook(hooks, u)

            def epilogue(kind, chunk, m, acc, done):
                def copy_out():
                    act.wait_ge(unit_done, UNITS * done)
                    summed = main[acc][:, :, :].rearrange("p h n -> p (h n)")
                    if kind == 1:
                        act.activation(rows[:, :, :], side[acc][:, :, :].rearrange("p h (t f) -> p (h t) f", f=P), ACT.Copy)
                    if kind == 2:
                        act.wait_ge(small_loaded, 48)
                        act.activation(turn[:, :], summed, ACT.Identity, bias=bias_sb[:, :]).then_inc(turn_ready, 1)
                    else:
                        act.activation(turn[:, :], summed, ACT.Copy).then_inc(turn_ready, 1)

                def norm_rows(tiles):
                    act.wait_ge(norm_ready, m - NC + 1)
                    for t in tiles:
                        to = features[:, 0, bass.ds(chunk * CHUNK + t * P, P)] if kind == 2 else rows[:, t, :]
                        done = act.activation(to, rows[:, t, :], ACT.Identity, bias=shift[:, t:t + 1],
                                              scale=rstd[:, t:t + 1])
                    done.then_inc(normed, 1)

                q = (1, 3) if kind == 2 and chunk == NC - 2 else (0, 1)
                norm = {} if kind == 1 else {q[0]: lambda: norm_rows(range(TILES // 2)),
                                             q[1]: lambda: norm_rows(range(TILES // 2, TILES))}
                return ({2: copy_out}, {}, {}, norm) if kind == 3 else ({2: copy_out}, {}, norm, {})

            act.dma_start(d_sb[:, :, :], d).then_inc(small_loaded, 16)
            act.dma_start(filt_sb[:, :, :], filt).then_inc(small_loaded, 16)
            act.dma_start(bias_sb[:, :], bias).then_inc(small_loaded, 16)

            def copy_turned(c):
                act.wait_ge(x_turned, c + 1)
                act.activation(turn[:, :], x_turned_bank, ACT.Copy).then_inc(x_turn_ready, 1)

            def copy_product(c):
                act.wait_ge(xw_summed, c + 1)
                act.activation(features[:, 0, c * CHUNK:(c + 1) * CHUNK], xw_bank, ACT.Copy).then_inc(xw_ready, 1)
                if c == NC - 1:
                    act.wait_ge(xw_ready, NC)
                    act.sem_inc(released, 1)

            def copy_xw(J):
                c = J + XW_AHEAD - 1
                if J == 0:
                    return {0: lambda: copy_turned(1), 3: lambda: copy_product(1)}
                return {1: lambda: copy_turned(c), 3: lambda: copy_product(c)} if c < NC else {}

            copy_turned(0)
            copy_product(0)
            act.wait_ge(side_zeroed, 1)
            walk(act, split, epilogue, copy_xw)

        @block.vector
        def _(dve):
            def split_features(phase, J, B, dual, half):
                ops = operands(phase, dual)
                dve.wait_ge(w_hi_ready, 2 * B + half + 1)
                dve.tensor_tensor(w_lo[:, half, ops, :],
                                  features[:, ops, bass.ds(J * CHUNK + half * HB, HB)],
                                  w_hi[:, half, ops, :].bitcast(F32), ALU.subtract).then_inc(w_lo_ready, 1)

            def split(phase, I, J, B, acc, dual, hooks, slot=None):
                which, used, _ = slot or (0, B, 1)
                for u in range(UNITS):
                    if u % HALF == 0:
                        split_features(phase, J, B, dual, u // HALF)
                    dve.wait_ge(hi_ready, UNITS * B + u + 1)
                    if not (is_first(B) and u < LO_RING):
                        dve.wait_ge(unit_done, UNITS * B + u + 1 - LO_RING)
                    dve.tensor_tensor(lo[:, u % LO_RING, :], slots[which][:, u, :], hi[:, u, :].bitcast(F32),
                                      ALU.subtract).then_inc(lo_ready, 1)
                    run_hook(hooks, u)

            def invert_degrees():
                deg = inv_deg[:, :]
                dve.tensor_reduce(deg, deg_parts[:, :, :].rearrange("p c t -> p t c"), AX.X,
                                  ALU.add).then_inc(deg_step, 1)
                dve.wait_ge(deg_step, 1)
                dve.scalar_tensor_tensor(out=abs_deg[:, :], in0=deg, scalar=-1.0, in1=deg, op0=ALU.mult,
                                         op1=ALU.max).then_inc(deg_step, 1)
                dve.wait_ge(deg_step, 2)
                dve.tensor_scalar(no_inv[:, :], abs_deg[:, :], LARGEST_WITHOUT_INVERSE, None,
                                  ALU.is_le).then_inc(deg_step, 1)
                dve.wait_ge(deg_step, 3)
                dve.copy_predicated(deg, no_inv[:, :], ones[:, :]).then_inc(deg_step, 1)
                dve.wait_ge(deg_step, 4)
                dve.reciprocal(inv_deg[:, :], deg).then_inc(deg_step, 1)
                dve.wait_ge(deg_step, 5)
                dve.copy_predicated(inv_deg[:, :], no_inv[:, :], zero_col[:, :]).then_inc(deg_step, 1)
                dve.wait_ge(deg_step, 6)

            def epilogue(kind, chunk, m, acc, done):
                def turned_rows(banks):
                    return banks[acc][:, :, :].rearrange("p h (t f) -> p (h t) f", f=P)

                tiles = bass.ds(chunk * TILES, TILES)
                columns = bass.ds(chunk * CHUNK, CHUNK)

                def per_row(column):
                    return column[:, tiles].unsqueeze(2).to_broadcast([P, TILES, P])

                def keep_rows():
                    dve.wait_ge(turned, m + 1)
                    dve.tensor_tensor(features[:, 1, columns].rearrange("p (t f) -> p t f", f=P),
                                      turned_rows(main), per_row(scale), ALU.mult).then_inc(scaled, 1)
                    kept = partial[:, columns].rearrange("p (t f) -> p t f", f=P)
                    dve.tensor_tensor(kept, turned_rows(side), kept, ALU.add).then_inc(released, 1)

                def add_up():
                    dve.wait_ge(turned, m + 1)
                    if kind == 2:
                        if chunk:
                            dve.wait_ge(normed, 2 * chunk)
                        dve.tensor_tensor(rows[:, :, :], turned_rows(main),
                                          partial[:, columns].rearrange("p (t f) -> p t f", f=P),
                                          ALU.add).then_inc(released, 1)
                    else:
                        dve.wait_ge(rows_free, chunk + 1)
                        dve.tensor_tensor(rows[:, :, :], turned_rows(main), per_row(inv_deg), ALU.mult)\
                           .then_inc(released, 1)

                def add_residual():
                    dve.wait_ge(released, m + 2)
                    dve.tensor_tensor(rows[:, :, :], rows[:, :, :],
                                      features[:, 0, columns].rearrange("p (t f) -> p t f", f=P),
                                      ALU.add).then_inc(residual_added, 1)

                def statistics(tiles):
                    if kind == 2:
                        dve.wait_ge(released, m + 2)
                    else:
                        dve.wait_ge(residual_added, chunk + 1)
                    for t in tiles:
                        done = dve.bn_stats(stats[:, t, :], rows[:, t, :])
                    done.then_inc(stats_ready, 1)

                first_half = lambda: statistics(range(TILES // 2))
                last_half = lambda: statistics(range(TILES // 2, TILES))
                if kind == 1:
                    return {3: keep_rows}, {}, {}, {}
                if kind == 3:
                    return {3: add_up}, {1: add_residual, 3: first_half}, {1: last_half}, {}
                if chunk == NC - 2:
                    return {3: lambda: (add_up(), first_half(), last_half())}, {}, {}, {}
                if chunk == NC - 1:
                    return {}, {0: add_up, 1: first_half, 2: last_half}, {3: invert_degrees}, {}
                return {3: add_up}, {0: first_half, 1: last_half}, {}, {}

            dve.memset(side[0][:, :, :], 0.0).then_inc(side_zeroed, 1)
            dve.wait_ge(small_loaded, 48)
            dve.tensor_tensor(filt_sb[:, :, :], d_sb[:, :, :], filt_sb[:, :, :], ALU.mult).then_inc(scale_step, 1)
            dve.wait_ge(scale_step, 1)
            dve.tensor_tensor(filt_sb[:, :, :], filt_sb[:, :, :], d_sb[:, :, :], ALU.mult).then_inc(scale_step, 1)
            dve.wait_ge(scale_step, 2)
            dve.tensor_tensor(scale[:, :], filt_sb[:, 0, :], filt_sb[:, 1, :], ALU.add).then_inc(scale_step, 1)
            for r in range(2, NR):
                dve.wait_ge(scale_step, r + 1)
                dve.tensor_tensor(scale[:, :], scale[:, :], filt_sb[:, r, :], ALU.add).then_inc(scale_step, 1)
            dve.wait_ge(scale_step, NR + 1)
            dve.wait_ge(consts_ready, CONSTS)
            walk(dve, split, epilogue)

        @block.tensor
        def _(pe):
            def multiply(phase, J, B, acc, dual, hooks, first):
                into = (main[acc], side[acc] if dual else None)
                for u in range(UNITS):
                    half, base = u // HALF, (u % HALF) * UNIT_TILES * P
                    weights = [[w[:, half, op, base + k * P:base + (k + 1) * P] for k in range(UNIT_TILES)]
                               for w in (w_hi, w_lo) for op in range(2)]
                    start = first and u == 0

                    def add(tile, w, start):
                        for n, op in enumerate((0, 1) if dual else (1,) if phase == 2 else (0,)):
                            for k in range(UNIT_TILES):
                                for b in range(HALVES):
                                    done = pe.matmul(into[n][:, b, :], weights[2 * w + op][k],
                                                     tile[:, k * CHUNK + b * BANK:k * CHUNK + (b + 1) * BANK],
                                                     start=start and k == 0, stop=False, skip_group_check=True)
                        return done

                    if u % HALF == 0:
                        pe.wait_ge(w_lo_ready, 2 * B + half + 1)
                    pe.wait_ge(hi_ready, UNITS * B + u + 1)
                    add(hi[:, u, :], 0, start)
                    add(hi[:, u, :], 1, False)
                    pe.wait_ge(lo_ready, UNITS * B + u + 1)
                    add(lo[:, u % LO_RING, :], 0, False).then_inc(unit_done, 1)
                    run_hook(hooks, u)

            def work(phase, I, J, B, acc, dual, hooks, slot=None):
                first = isinstance(J, int) and J == (0 if phase == 3 else I)
                if first:
                    n = NC * (phase - 1) + (0 if phase == 2 and I == 1 else I)
                    if not is_first(n):
                        pe.wait_ge(released, n)
                    if phase == 1 and not (isinstance(I, int) and I == 0):
                        for b in range(HALVES):
                            pe.matmul(side[acc][:, b, :], zeros[:, 0:P], zeros[:, :], start=True, stop=False,
                                      skip_group_check=True)
                multiply(phase, J, B, acc, dual, hooks, first)

            def epilogue(kind, chunk, m, acc, done):
                def transpose():
                    pe.wait_ge(turn_ready, m + 1)
                    pairs = ((side, rows[:, :, :].rearrange("p t f -> p (t f)")),) if kind == 1 else ()
                    for banks, source in (*pairs, (main, turn[:, :])):
                        for h in range(HALVES):
                            for t in range(BANK // P):
                                done = pe.transpose(banks[acc][:, h, t * P:(t + 1) * P],
                                                    source[:, h * BANK + t * P:h * BANK + (t + 1) * P], ident[:, :])
                    done.then_inc(turned, 1)

                return {1: transpose}, {}, {}, {}

            def turn_x(c):
                pe.wait_ge(x_loaded[c], 16)
                if c:
                    pe.wait_ge(x_turn_ready, c)
                for t in range(TILES):
                    at = slice(t * P, (t + 1) * P)
                    done = pe.transpose(x_turned_bank[:, at], partial[:, c * CHUNK + t * P:c * CHUNK + (t + 1) * P],
                                        ident[:, :])
                done.then_inc(x_turned, 1)

            def multiply_x(c):
                pe.wait_ge(x_turn_ready, c + 1)
                if c:
                    pe.wait_ge(xw_ready, c)
                for t in range(TILES):
                    at = slice(t * P, (t + 1) * P)
                    done = pe.matmul(xw_bank[:, at], turn[:, at], w_sb[:, :], start=True, stop=True,
                                     skip_group_check=True)
                done.then_inc(xw_summed, 1)

            def multiply_xw(J):
                c = J + XW_AHEAD
                if J == 0:
                    return {0: lambda: multiply_x(1), 2: lambda: turn_x(2), 3: lambda: multiply_x(2)}
                return {1: lambda: turn_x(c), 3: lambda: multiply_x(c)} if c < NC else {}

            pe.wait_ge(consts_ready, CONSTS)
            pe.wait_ge(w_loaded, 16)
            turn_x(0)
            multiply_x(0)
            turn_x(1)
            walk(pe, work, epilogue, multiply_xw)


def kernel(x, adj, L0_gnn_d_list, L0_gnn_weight, L0_gnn_filt, L0_gnn_bias):
    import numpy as np
    import concourse.bacc as bacc
    from concourse.bass_utils import run_bass_kernel_spmd

    def by_row_tile(a):
        a = np.asarray(a)
        return np.ascontiguousarray(a.reshape(a.shape[0], -1, P).transpose(2, 0, 1))

    x, adj, bias = np.asarray(x), np.asarray(adj), np.asarray(L0_gnn_bias)
    arrays = {
        "x": np.ascontiguousarray(x),
        "A": np.ascontiguousarray(adj),
        "AT": np.ascontiguousarray(adj.T),
        "d": by_row_tile(L0_gnn_d_list),
        "filt": by_row_tile(L0_gnn_filt),
        "weight": np.ascontiguousarray(np.asarray(L0_gnn_weight)),
        "bias": np.ascontiguousarray(bias.reshape(P, 1)),
    }
    nc = bacc.Bacc("TRN2", target_bir_lowering=False, num_devices=1)
    args = [nc.dram_tensor(name, a.shape, F32, kind="ExternalInput").ap() for name, a in arrays.items()]
    out = nc.dram_tensor("out", x.shape, F32, kind="ExternalOutput").ap()
    build(nc, *args, out)
    r = run_bass_kernel_spmd(nc, [arrays], core_ids=[0])
    return r.results[0]["out"]
```
